# Optimizing a Trainium2 kernel written in Bass

```python
import numpy as np
import jax
import jax.numpy as jnp

def _softmax(x, axis=-1):
    return jax.nn.softmax(x, axis=axis)

def _gelu(x):
    return jax.nn.gelu(x, approximate=True)

def _silu(x):
    return jax.nn.silu(x)

def _sigmoid(x):
    return jax.nn.sigmoid(x)

def _layernorm(x, axis=-1, eps=1e-05):
    m = jnp.mean(x, axis=axis, keepdims=True)
    v = jnp.var(x, axis=axis, keepdims=True)
    return (x - m) / jnp.sqrt(v + eps)

def _scatter_add(tgt, idx, src, axis=0):
    return tgt.at[idx].add(src)

def _segment_sum(src, seg, n):
    return jax.ops.segment_sum(src, seg, n)
kernel_name = 'mk_conv_preact_d1_conv_nchw2048_r2_a66e94'

def setup_inputs(seed: int=0):
    np.random.seed(seed)
    _w = jnp.asarray

    def _rec_inputs():
        import jax
        import jax.numpy as jnp
        _gk = jax.random.key(seed)
        x = -9.26e-05 + 0.9999 * jax.random.normal(jax.random.fold_in(_gk, 1), (4, 1024, 48, 48), jnp.float32)
        return x
    x = _rec_inputs()

    def _L0_conv_setup():
        import jax, jax.numpy as jnp
        import numpy as np
        N, C, H, WD = (4, 1024, 48, 48)
        KH = 9
        key = jax.random.key(seed)
        k1, k2, k3 = jax.random.split(key, 3)
        fea = jax.random.normal(k1, (N, C, H, WD), dtype=jnp.float32)
        W = jax.random.normal(k2, (C, C, KH, 1), dtype=jnp.float32) * 0.01
        b = jax.random.normal(k3, (C,), dtype=jnp.float32) * 0.01
        return {'fea': fea, 'W': W, 'b': b}
    _L0_conv_all = _L0_conv_setup()
    _L0_conv_in = {k: v for k, v in _L0_conv_all.items() if k in ('W', 'b')}
    del _L0_conv_all
    return {'x': x, 'L0_conv_W': _L0_conv_in['W'], 'L0_conv_b': _L0_conv_in['b']}

def reference(x, L0_conv_W, L0_conv_b):
    import jax
    import jax.numpy as jnp

    def _L0_conv_ref(fea, W, b):
        import jax, jax.numpy as jnp
        import numpy as np
        N, C, H, WD = (4, 1024, 48, 48)
        KH = 9
        kh = W.shape[2]
        Wm = W[:, :, (kh - 1) // 2, 0]
        bb = b[None, :, None]

        def step(carry, x):
            new = jax.nn.relu(jnp.einsum('oc,ncw->now', Wm, carry) + bb) + x
            return (new, new)
        xs = jnp.moveaxis(fea, 2, 0)
        _, ys = jax.lax.scan(step, xs[0], xs[1:])
        down = jnp.concatenate([xs[:1], ys], axis=0)
        _, ys2 = jax.lax.scan(step, down[-1], down[:-1], reverse=True)
        stack = jnp.concatenate([ys2, down[-1:]], axis=0)
        return jnp.moveaxis(stack, 0, 2)

    def _gn(v, G=32, eps=1e-05):
        B_, C_, H_, W_ = v.shape
        g = v.reshape(B_, G, C_ // G, H_, W_)
        m = jnp.mean(g, axis=(2, 3, 4), keepdims=True)
        s = jnp.var(g, axis=(2, 3, 4), keepdims=True)
        return ((g - m) / jnp.sqrt(s + eps)).reshape(v.shape)

    def _ln_c(v, eps=1e-06):
        m = jnp.mean(v, axis=1, keepdims=True)
        s = jnp.var(v, axis=1, keepdims=True)
        return (v - m) / jnp.sqrt(s + eps)

    def _ln_t(v, eps=1e-05):
        m = jnp.mean(v, axis=-1, keepdims=True)
        s = jnp.var(v, axis=-1, keepdims=True)
        return (v - m) / jnp.sqrt(s + eps)

    def _to_tokens(v):
        B_, C_, H_, W_ = v.shape
        return v.reshape(B_, C_, H_ * W_).transpose(0, 2, 1)

    def _from_tokens(t, like):
        B_, C_, H_, W_ = like.shape
        return t.transpose(0, 2, 1).reshape(B_, C_, H_, W_)
    x = x + _L0_conv_ref(_gn(x), L0_conv_W, L0_conv_b)
    return x

_drawn_inputs = setup_inputs


def setup_inputs(seed=0):
    import zlib

    import numpy as np

    out = dict(_drawn_inputs(seed))
    spreads = {}
    factors = {'L0_conv_b': 8.0}
    for name, (base, spread) in spreads.items():
        noise = np.random.default_rng([zlib.crc32(name.encode()), seed]).standard_normal(out[name].shape)
        drawn = base * np.exp(spread * noise) if base else spread * noise
        out[name] = jnp.asarray(drawn.astype(out[name].dtype))
    for name, factor in factors.items():
        out[name] = (out[name] * factor).astype(out[name].dtype)
    return out
```

```python
from contextlib import ExitStack

import numpy as np

import concourse.bass as bass
from concourse import mybir
from concourse.alu_op_type import AluOpType as ALU

F32 = mybir.dt.float32
F32R = mybir.dt.float32r
ACT = mybir.ActivationFunctionType

P = 128
SLOTS = 8
GN_GROUP = 32
GN_EPS = 1e-5
STAT_CHUNKS = 4
BN_DIM = 6


def build(nc, x_rows, w_t, bias, down_rows, out_rows):
    H, _, row_elems = x_rows.shape
    K = w_t.shape[0]
    C = w_t.shape[2]
    NI = 4
    COLS = row_elems // K
    WIDTH = COLS // NI
    GROUPS = H // SLOTS
    STEPS = 2 * (H - 1)
    TC = K // STAT_CHUNKS
    assert H % SLOTS == 0 and STEPS % 2 == 0 and C == K * P and 2 * COLS <= 512

    with ExitStack() as ctx:
        def sb(name, shape, dt=F32):
            return ctx.enter_context(nc.sbuf_tensor(name, shape, dt))

        def sem(name):
            return ctx.enter_context(nc.semaphore(name))

        w_hi = sb("w_hi", [P, K, C], F32R)
        w_lo = sb("w_lo", [P, K, C], F32R)
        carry = sb("carry", [P, 2, K, 2, COLS], F32R)
        xn = sb("xn", [P, 2, K * COLS])
        x_ring = sb("x_ring", [P, SLOTS, K * COLS])
        d_ring = sb("d_ring", [P, SLOTS, K * COLS])
        work = sb("work", [P, K * COLS])
        summed = sb("summed", [P, 2, COLS])
        bias_sb = sb("bias_sb", [P, K])
        group_avg = sb("group_avg", [P, P])
        moments = sb("moments", [P, K * NI, 2])
        delta = sb("delta", [P, K * NI])
        spread = sb("spread", [P, K * NI])
        gn_mean = sb("gn_mean", [P, K * NI])
        gn_std = sb("gn_std", [P, K * NI])
        gn_rstd = sb("gn_rstd", [P, K * NI])
        eps = sb("eps", [P, 1])

        bank = [ctx.enter_context(nc.psum_tensor(f"bank{m}", [P, 512], F32)) for m in range(K)]

        bn = work[:, 0:K * NI * GROUPS * BN_DIM].rearrange("p (c s) -> p c s", c=K * NI)
        act_part = work[:, :].rearrange("p (m c) -> p m c", m=K)

        def tile(ring, slot, k):
            return ring[:, slot, k * COLS:(k + 1) * COLS]

        def by_image(ap):
            return ap.rearrange("p (n w) -> p n w", w=WIDTH)

        def spread_over_width(table, k):
            return table[:, k * NI:(k + 1) * NI].unsqueeze(2).broadcast_to([P, NI, WIDTH])

        stat_loaded = [[sem(f"stat_loaded{a}_{c}") for c in range(STAT_CHUNKS)] for a in range(2)]
        bias_loaded = sem("bias_loaded")
        w_loaded = [sem(f"w_loaded{i}") for i in range(2)]
        w_hi_ready = sem("w_hi_ready")
        w_lo_ready = sem("w_lo_ready")
        stats_done = sem("stats_done")
        const_ready = sem("const_ready")
        bn_step = sem("bn_step")
        moments_ready = sem("moments_ready")
        mean_summed = sem("mean_summed")
        spread_ready = sem("spread_ready")
        var_summed = sem("var_summed")
        std_ready = sem("std_ready")
        gn_ready = sem("gn_ready")
        x_loaded = [sem(f"x_loaded{j}") for j in range(SLOTS)]
        d_loaded = [sem(f"d_loaded{j}") for j in range(SLOTS)]
        d_stored = [sem(f"d_stored{j}") for j in range(SLOTS)]
        out_stored = [sem(f"out_stored{j}") for j in range(SLOTS)]
        centred = sem("centred")
        xn_ready = sem("xn_ready")
        psum_ready = sem("psum_ready")
        act_ready = sem("act_ready")
        sum_ready = sem("sum_ready")
        row_ready = sem("row_ready")
        hi_ready = sem("hi_ready")
        carry_ready = sem("carry_ready")
        out_ready = sem("out_ready")

        block = ctx.enter_context(nc.Block())


        @block.sync
        def _(sp):
            for g in range(GROUPS):
                area = g % 2
                ring = (d_ring, x_ring)[area]
                h0 = H - SLOTS * (g + 1)
                for c in range(STAT_CHUNKS):
                    if g >= 2:
                        sp.wait_ge(stats_done, (g - 2) * STAT_CHUNKS + c + 1)
                    cols = slice(c * TC * COLS, (c + 1) * TC * COLS)
                    sp.dma_start(ring[:, :, cols],
                                 x_rows[h0:h0 + SLOTS, :, cols].rearrange("h p e -> p h e")
                                 ).then_inc(stat_loaded[area][c], 16)

            def down_row(g, j, load, store):
                h = SLOTS * g + j
                if load:
                    sp.wait_ge(xn_ready, K * h + K)
                    sp.dma_start(x_ring[:, j, :], x_rows[bass.ds(h + SLOTS, 1), :, :].rearrange("o p e -> p (o e)")
                                 ).then_inc(x_loaded[j], 16)
                if store:
                    sp.wait_ge(row_ready, K * h + K)
                    sp.dma_start(down_rows[bass.ds(h, 1), :, :].rearrange("o p e -> p (o e)"), d_ring[:, j, :]
                                 ).then_inc(d_stored[j], 16)

            with sp.Fori(0, GROUPS - 1) as g:
                for j in range(SLOTS):
                    down_row(g, j, True, True)

            def up_row(back, j, load_x, load_d):
                done = SLOTS * back + SLOTS - j
                h = (back * -SLOTS) + (H - SLOTS + j)
                sp.wait_ge(out_ready, K * done)
                sp.dma_start(out_rows[bass.ds(h, 1), :, :].rearrange("o p e -> p (o e)"), x_ring[:, j, :]
                             ).then_inc(out_stored[j], 16)
                if load_d:
                    if back is first_back:
                        sp.wait_ge(d_stored[j], 16 * (GROUPS - 1))
                    sp.dma_start(d_ring[:, j, :],
                                 down_rows[bass.ds(h - SLOTS, 1), :, :].rearrange("o p e -> p (o e)")
                                 ).then_inc(d_loaded[j], 16)
                if load_x:
                    above = (j + 1) % SLOTS
                    stored = back + 1 if j < SLOTS - 1 else back
                    sp.wait_ge(out_stored[above], 16 * stored)
                    sp.dma_start(x_ring[:, above, :],
                                 x_rows[bass.ds(h + 1 - SLOTS, 1), :, :].rearrange("o p e -> p (o e)")
                                 ).then_inc(x_loaded[above], 16)

            first_back = 0
            for j in reversed(range(SLOTS)):
                up_row(first_back, j, j < SLOTS - 1, True)
            with sp.Fori(1, GROUPS - 1) as back:
                for j in reversed(range(SLOTS)):
                    up_row(back, j, True, True)
            for j in reversed(range(SLOTS)):
                up_row(GROUPS - 1, j, j == SLOTS - 1, False)
            for j in range(SLOTS):
                sp.wait_ge(out_stored[j], 16 * GROUPS)

        @block.gpsimd
        def _(pool):
            for k in range(K):
                pool.wait_ge(w_hi_ready, k + 1)
                pool.tensor_tensor(w_lo[:, k, :], xn[:, k % 2, 0:C], w_hi[:, k, :].bitcast(F32),
                                   ALU.subtract).then_inc(w_lo_ready, 1)
            pool.wait_ge(w_lo_ready, K)
            pool.wait_ge(gn_ready, 1)

            def normalise(g, j, reused):
                h = SLOTS * g + j
                pool.wait_ge(x_loaded[j], 16 * g)
                for k in range(K):
                    if reused:
                        pool.wait_ge(row_ready, K * (h - 2) + k + 1)
                    dst = by_image(tile(xn, j % 2, k))
                    pool.tensor_tensor(dst, by_image(tile(x_ring, j, k)), spread_over_width(gn_mean, k),
                                       ALU.subtract).then_inc(centred, 1)
                    pool.wait_ge(centred, K * h + k + 1)
                    pool.tensor_tensor(dst, dst, spread_over_width(gn_rstd, k), ALU.mult).then_inc(xn_ready, 1)

            for j in range(SLOTS):
                normalise(0, j, j >= 2)
            with pool.Fori(1, GROUPS) as g:
                for j in range(SLOTS):
                    normalise(g, j, True)

            def output(back, j, loaded):
                done = SLOTS * back + SLOTS - j
                if loaded:
                    pool.wait_ge(x_loaded[j], 16 * (GROUPS - 1 + back))
                for k in range(K):
                    pool.wait_ge(carry_ready, K * (H - 2 + done) + k + 1)
                    pool.tensor_tensor(tile(x_ring, j, k), tile(x_ring, j, k), tile(d_ring, j, k),
                                       ALU.add).then_inc(out_ready, 1)

            for j in reversed(range(SLOTS)):
                output(0, j, False)
            with pool.Fori(1, GROUPS) as back:
                for j in reversed(range(SLOTS)):
                    output(back, j, True)

        @block.scalar
        def _(act):
            act.dma_start(bias_sb[:, :], bias).then_inc(bias_loaded, 16)
            for k in range(2):
                act.dma_start(xn[:, k, 0:C], w_t[k]).then_inc(w_loaded[k], 16)
            for k in range(K):
                act.wait_ge(w_loaded[k % 2], 16 * (k // 2 + 1))
                act.activation(w_hi[:, k, :], xn[:, k % 2, 0:C], ACT.Copy).then_inc(w_hi_ready, 1)
                if k + 2 < K:
                    act.wait_ge(w_lo_ready, k + 1)
                    act.dma_start(xn[:, k % 2, 0:C], w_t[k + 2]).then_inc(w_loaded[k % 2], 16)
            act.wait_ge(const_ready, 1)
            act.wait_ge(var_summed, 1)
            act.activation(gn_std[:, :], bank[1][:, 0:K * NI], ACT.Sqrt, bias=eps[:, 0:1]).then_inc(std_ready, 1)
            act.wait_ge(bias_loaded, 16)

            with act.Fori(0, STEPS) as s:
                for m in range(K):
                    act.wait_ge(psum_ready, K * s + m + 1)
                    act.activation(act_part[:, m, :], bank[m][:, COLS:2 * COLS], ACT.Identity,
                                   bias=bias_sb[:, m:m + 1]).then_inc(act_ready, 1)

        @block.vector
        def _(dve):
            dve.memset(group_avg[:, :], 0.0).then_inc(bn_step, 1)
            dve.wait_ge(bn_step, 1)
            for q in range(0, P, GN_GROUP):
                dve.memset(group_avg[q:q + GN_GROUP, q:q + GN_GROUP], 1.0 / GN_GROUP)
            dve.memset(eps[:, :], GN_EPS).then_inc(const_ready, 1)

            for g in range(GROUPS):
                area = g % 2
                ring = (d_ring, x_ring)[area]
                for c in range(STAT_CHUNKS):
                    dve.wait_ge(stat_loaded[area][c], 16 * (g // 2 + 1))
                    for i in range(c * TC * NI, (c + 1) * TC * NI):
                        last = dve.bn_stats(bn[:, i, g * BN_DIM:(g + 1) * BN_DIM],
                                            ring[:, :, i * WIDTH:(i + 1) * WIDTH])
                    last.then_inc(stats_done, 1)
                    if g == GROUPS - 1:
                        dve.wait_ge(stats_done, g * STAT_CHUNKS + c + 1)
                        for i in range(c * TC * NI, (c + 1) * TC * NI):
                            last = dve.bn_aggr(moments[:, i, :], bn[:, i, :])
                        last.then_inc(moments_ready, 1)
            dve.wait_ge(mean_summed, 1)
            dve.tensor_copy(gn_mean[:, :], bank[0][:, 0:K * NI]).then_inc(bn_step, 1)
            dve.wait_ge(bn_step, 2)
            dve.wait_ge(moments_ready, STAT_CHUNKS)
            dve.tensor_tensor(delta[:, :], moments[:, :, 0], gn_mean[:, :], ALU.subtract).then_inc(bn_step, 1)
            dve.wait_ge(bn_step, 3)
            dve.tensor_tensor(spread[:, :], delta[:, :], delta[:, :], ALU.mult).then_inc(bn_step, 1)
            dve.wait_ge(bn_step, 4)
            dve.tensor_tensor(spread[:, :], spread[:, :], moments[:, :, 1], ALU.add).then_inc(spread_ready, 1)
            dve.wait_ge(std_ready, 1)
            dve.reciprocal(gn_rstd[:, :], gn_std[:, :]).then_inc(gn_ready, 1)

            def split(row, parity, j, m):
                dve.wait_ge(row_ready, K * row + m + 1)
                dve.tensor_copy(carry[:, parity, m, 0, :], tile(d_ring, j, m)).then_inc(hi_ready, 1)
                dve.wait_ge(hi_ready, K * row + m + 1)
                dve.tensor_tensor(carry[:, parity, m, 1, :], tile(d_ring, j, m),
                                  carry[:, parity, m, 0, :].bitcast(F32), ALU.subtract).then_inc(carry_ready, 1)

            for m in range(K):
                dve.wait_ge(xn_ready, m + 1)
                dve.tensor_copy(tile(d_ring, 0, m), tile(xn, 0, m)).then_inc(row_ready, 1)
                split(0, 0, 0, m)

            def row_tiles(row, j, parity, addend):
                for m in range(K):
                    n = K * (row - 1) + m
                    dve.wait_ge(act_ready, n + 1)
                    dve.tensor_tensor(summed[:, m % 2, :], bank[m][:, 0:COLS], act_part[:, m, :],
                                      ALU.add).then_inc(sum_ready, 1)
                    dve.wait_ge(sum_ready, n + 1)
                    dve.scalar_tensor_tensor(out=tile(d_ring, j, m), in0=summed[:, m % 2, :], scalar=0.0,
                                             in1=addend(m), op0=ALU.max, op1=ALU.add).then_inc(row_ready, 1)
                    split(row, parity, j, m)

            def down_row(g, j):
                h = SLOTS * g + j
                dve.wait_ge(xn_ready, K * h + K)
                dve.wait_ge(d_stored[j], 16 * g)
                row_tiles(h, j, j % 2, lambda m: tile(xn, j % 2, m))

            for j in range(1, SLOTS):
                down_row(0, j)
            with dve.Fori(1, GROUPS) as g:
                for j in range(SLOTS):
                    down_row(g, j)

            def up_row(back, j, loaded):
                row = H - 1 + SLOTS * back + SLOTS - 1 - j
                if loaded:
                    dve.wait_ge(d_loaded[j], 16 * back)
                row_tiles(row, j, j % 2, lambda m: tile(d_ring, j, m))

            for j in reversed(range(SLOTS - 1)):
                up_row(0, j, False)
            with dve.Fori(1, GROUPS) as back:
                for j in reversed(range(SLOTS)):
                    up_row(back, j, True)

        @block.tensor
        def _(pe):
            pe.wait_ge(const_ready, 1)
            pe.wait_ge(moments_ready, STAT_CHUNKS)
            pe.matmul(bank[0][:, 0:K * NI], group_avg[:, :], moments[:, :, 0],
                      start=True, stop=True).then_inc(mean_summed, 1)
            pe.wait_ge(spread_ready, 1)
            pe.matmul(bank[1][:, 0:K * NI], group_avg[:, :], spread[:, :],
                      start=True, stop=True).then_inc(var_summed, 1)
            pe.wait_ge(w_lo_ready, K)

            def product(parity, m, k):
                out_cols = slice(m * P, (m + 1) * P)
                pe.matmul(bank[m][:, 0:2 * COLS], w_hi[:, k, out_cols],
                          carry[:, parity, k, :, :].rearrange("p s c -> p (s c)"), start=(k == 0), stop=False)
                last = pe.matmul(bank[m][:, 0:COLS], w_lo[:, k, out_cols], carry[:, parity, k, 0, :],
                                 start=False, stop=(k == K - 1))
                if k == K - 1:
                    last.then_inc(psum_ready, 1)

            with pe.Fori(0, STEPS // 2) as pair:
                for parity in range(2):
                    done = K * (2 * pair + parity)
                    pe.wait_ge(carry_ready, done + K - 2)
                    for k in range(K - 2):
                        product(parity, 0, k)
                    pe.wait_ge(carry_ready, done + K - 1)
                    product(parity, 0, K - 2)
                    for k in range(K - 1):
                        product(parity, 1, k)
                    pe.wait_ge(carry_ready, done + K)
                    product(parity, 0, K - 1)
                    product(parity, 1, K - 1)
                    for m in range(2, K):
                        for k in range(K):
                            product(parity, m, k)


def kernel(x, L0_conv_W, L0_conv_b):
    import concourse.bacc as bacc
    from concourse.bass_utils import run_bass_kernel_spmd

    x, w, b = np.asarray(x), np.asarray(L0_conv_W), np.asarray(L0_conv_b)
    N, C, H, W = x.shape
    K = C // P
    tap = (w.shape[2] - 1) // 2
    x_rows = np.ascontiguousarray(x.reshape(N, K, P, H, W).transpose(3, 2, 1, 0, 4)).reshape(H, P, K * N * W)
    w_t = np.ascontiguousarray(w[:, :, tap, 0].T).reshape(K, P, C)
    bias = np.ascontiguousarray(b.reshape(K, P).T)

    nc = bacc.Bacc("TRN2", target_bir_lowering=False, num_devices=1)
    arrays = {"x_rows": x_rows, "w_t": w_t, "bias": bias}
    ins = [nc.dram_tensor(name, a.shape, F32, kind="ExternalInput").ap() for name, a in arrays.items()]
    down_rows = nc.dram_tensor("down_rows", x_rows.shape, F32, kind="Internal").ap()
    out_rows = nc.dram_tensor("out_rows", x_rows.shape, F32, kind="ExternalOutput").ap()
    build(nc, *ins, down_rows, out_rows)
    got = run_bass_kernel_spmd(nc, [arrays], core_ids=[0]).results[0]["out_rows"]
    return np.ascontiguousarray(got.reshape(H, P, K, N, W).transpose(3, 2, 1, 0, 4)).reshape(N, C, H, W)
```

```python
from contextlib import ExitStack

import numpy as np

import concourse.bass as bass
from concourse import mybir
from concourse.alu_op_type import AluOpType as ALU

F32 = mybir.dt.float32
F32R = mybir.dt.float32r
ACT = mybir.ActivationFunctionType

P = 128
SLOTS = 8
GN_GROUP = 32
GN_EPS = 1e-5
STAT_CHUNKS = 4
DVE_LO = 2
WAVE = 6
WAVE_1 = 5
BN_DIM = 6


def build(nc, x_rows, w_t, bias, down_rows, out_rows):
    H, _, row_elems = x_rows.shape
    K = w_t.shape[0]
    C = w_t.shape[2]
    NI = 4
    COLS = row_elems // K
    WIDTH = COLS // NI
    GROUPS = H // SLOTS
    STEPS = 2 * (H - 1)
    TC = K // STAT_CHUNKS
    LAST = GROUPS - 1
    assert WAVE <= K - DVE_LO
    assert GROUPS % 2 == 0 and K == SLOTS
    assert H % SLOTS == 0 and STEPS % 2 == 0 and C == K * P and 2 * COLS <= 512

    with ExitStack() as ctx:
        def sb(name, shape, dt=F32):
            return ctx.enter_context(nc.sbuf_tensor(name, shape, dt))

        def sem(name):
            return ctx.enter_context(nc.semaphore(name))

        w_hi = sb("w_hi", [P, K, C], F32R)
        w_lo = sb("w_lo", [P, K, C], F32R)
        carry = sb("carry", [P, 2, K, 2, COLS], F32R)
        xn = sb("xn", [P, 2, K * COLS])
        x_ring = sb("x_ring", [P, SLOTS, K * COLS])
        d_ring = sb("d_ring", [P, SLOTS, K * COLS])
        work = sb("work", [P, K * COLS])
        summed = sb("summed", [P, 2, COLS])
        bias_sb = sb("bias_sb", [P, K])
        group_avg = sb("group_avg", [P, P])
        moments = sb("moments", [P, K * NI, 2])
        delta = sb("delta", [P, K * NI])
        spread = sb("spread", [P, K * NI])
        gn_mean = sb("gn_mean", [P, K * NI])
        gn_std = sb("gn_std", [P, K * NI])
        gn_rstd = sb("gn_rstd", [P, K * NI])
        eps = sb("eps", [P, 1])
        table_probe = sb("table_probe", [P, 1])

        bank = [ctx.enter_context(nc.psum_tensor(f"bank{m}", [P, 512], F32)) for m in range(K)]

        bn = work[:, 0:K * NI * GROUPS * BN_DIM].rearrange("p (c s) -> p c s", c=K * NI)
        act_part = work[:, :].rearrange("p (m c) -> p m c", m=K)

        def tile(ring, slot, k):
            return ring[:, slot, k * COLS:(k + 1) * COLS]

        w_raw = [d_ring[:, k + 1, 0:C] for k in range(K - 1)] + [xn[:, 0, 0:C]]

        def by_image(ap):
            return ap.rearrange("p (n w) -> p n w", w=WIDTH)

        def spread_over_width(table, k):
            return table[:, k * NI:(k + 1) * NI].unsqueeze(2).broadcast_to([P, NI, WIDTH])

        stat_loaded = [[sem(f"stat_loaded{a}_{c}") for c in range(STAT_CHUNKS)] for a in range(2)]
        last_loaded = [sem(f"last_loaded{k}") for k in range(K)]
        bias_loaded = sem("bias_loaded")
        w_loaded = [sem(f"w_loaded{k}") for k in range(K)]
        w_hi_ready = sem("w_hi_ready")
        w_lo_ready = sem("w_lo_ready")
        w_lo_rest_ready = sem("w_lo_rest_ready")
        stats_done = sem("stats_done")
        const_ready = sem("const_ready")
        bn_step = sem("bn_step")
        moments_ready = sem("moments_ready")
        mean_summed = sem("mean_summed")
        spread_ready = sem("spread_ready")
        var_summed = sem("var_summed")
        std_ready = sem("std_ready")
        gn_ready = sem("gn_ready")
        x_loaded = [sem(f"x_loaded{j}") for j in range(SLOTS)]
        d_loaded = [sem(f"d_loaded{j}") for j in range(SLOTS)]
        d_stored = [sem(f"d_stored{j}") for j in range(SLOTS)]
        out_stored = [sem(f"out_stored{j}") for j in range(SLOTS)]
        centred = sem("centred")
        xn_ready = sem("xn_ready")
        psum_ready = sem("psum_ready")
        act_ready = sem("act_ready")
        sum_ready = sem("sum_ready")
        row_ready = sem("row_ready")
        hi_ready = sem("hi_ready")
        carry_ready = sem("carry_ready")
        out_ready = sem("out_ready")

        block = ctx.enter_context(nc.Block())


        @block.sync
        def _(sp):
            for g in range(LAST):
                area = g % 2
                ring = (d_ring, x_ring)[area]
                h0 = H - SLOTS * (g + 1)
                for c in range(STAT_CHUNKS):
                    if g >= 2:
                        sp.wait_ge(stats_done, (g - 2) * STAT_CHUNKS + c + 1)
                    cols = slice(c * TC * COLS, (c + 1) * TC * COLS)
                    sp.dma_start(ring[:, :, cols],
                                 x_rows[h0:h0 + SLOTS, :, cols].rearrange("h p e -> p h e")
                                 ).then_inc(stat_loaded[area][c], 16)
            for k in range(K):
                if k % TC == 0:
                    sp.wait_ge(stats_done, (LAST - 2) * STAT_CHUNKS + k // TC + 1)
                cols = slice(k * COLS, (k + 1) * COLS)
                sp.dma_start(x_ring[:, :, cols], x_rows[0:SLOTS, :, cols].rearrange("h p e -> p h e")
                             ).then_inc(last_loaded[k], 16)
            sp.wait_ge(stats_done, LAST * STAT_CHUNKS)
            for k in range(K):
                sp.dma_start(w_raw[k], w_t[k]).then_inc(w_loaded[k], 16)

            def down_row(g, j, load, store):
                h = SLOTS * g + j
                if load:
                    sp.wait_ge(xn_ready, K * h)
                    sp.dma_start(x_ring[:, j, :], x_rows[bass.ds(h + SLOTS, 1), :, :].rearrange("o p e -> p (o e)")
                                 ).then_inc(x_loaded[j], 16)
                if store:
                    sp.wait_ge(row_ready, K * h + K)
                    sp.dma_start(down_rows[bass.ds(h, 1), :, :].rearrange("o p e -> p (o e)"), d_ring[:, j, :]
                                 ).then_inc(d_stored[j], 16)

            sp.wait_ge(row_ready, K)
            with sp.Fori(0, GROUPS - 1) as g:
                for j in range(SLOTS):
                    down_row(g, j, True, True)

            def up_row(back, j, load_x, load_d):
                done = SLOTS * back + SLOTS - j
                h = (back * -SLOTS) + (H - SLOTS + j)
                sp.wait_ge(out_ready, K * done)
                sp.dma_start(out_rows[bass.ds(h, 1), :, :].rearrange("o p e -> p (o e)"), x_ring[:, j, :]
                             ).then_inc(out_stored[j], 16)
                if load_d:
                    if back is first_back:
                        sp.wait_ge(d_stored[j], 16 * (GROUPS - 1))
                    sp.dma_start(d_ring[:, j, :],
                                 down_rows[bass.ds(h - SLOTS, 1), :, :].rearrange("o p e -> p (o e)")
                                 ).then_inc(d_loaded[j], 16)
                if load_x:
                    above = (j + 1) % SLOTS
                    stored = back + 1 if j < SLOTS - 1 else back
                    sp.wait_ge(out_stored[above], 16 * stored)
                    sp.dma_start(x_ring[:, above, :],
                                 x_rows[bass.ds(h + 1 - SLOTS, 1), :, :].rearrange("o p e -> p (o e)")
                                 ).then_inc(x_loaded[above], 16)

            first_back = 0
            for j in reversed(range(SLOTS)):
                up_row(first_back, j, j < SLOTS - 1, True)
            with sp.Fori(1, GROUPS - 1) as back:
                for j in reversed(range(SLOTS)):
                    up_row(back, j, True, True)
            for j in reversed(range(1, SLOTS)):
                up_row(GROUPS - 1, j, j == SLOTS - 1, False)
            for k in range(K):
                sp.wait_ge(out_ready, K * (H - 1) + k + 1)
                sp.dma_start(out_rows[0, :, k * COLS:(k + 1) * COLS], tile(x_ring, 0, k)).then_inc(out_stored[0], 16)
            sp.wait_ge(out_stored[0], 16 * (GROUPS - 1 + K))
            for j in range(1, SLOTS):
                sp.wait_ge(out_stored[j], 16 * GROUPS)

        @block.gpsimd
        def _(pool):
            for k in range(K - DVE_LO):
                pool.wait_ge(w_hi_ready, k + 1)
                pool.tensor_tensor(w_lo[:, k, :], w_raw[k], w_hi[:, k, :].bitcast(F32),
                                   ALU.subtract).then_inc(w_lo_ready, 1)
            pool.wait_ge(gn_ready, 1)

            def normalise(g, j, reloaded, reused):
                h = SLOTS * g + j
                if reloaded:
                    pool.wait_ge(x_loaded[j], 16 * g)
                for k in range(K):
                    if reused:
                        pool.wait_ge(row_ready, K * (h - 2) + k + 1)
                    dst = by_image(tile(xn, j % 2, k))
                    pool.tensor_tensor(dst, by_image(tile(x_ring, j, k)), spread_over_width(gn_mean, k),
                                       ALU.subtract).then_inc(centred, 1)
                    pool.wait_ge(centred, K * (h - 1) + k + 1)
                    pool.tensor_tensor(dst, dst, spread_over_width(gn_rstd, k), ALU.mult).then_inc(xn_ready, 1)

            for j in range(1, SLOTS):
                if j == 2:
                    pool.wait_ge(w_lo_rest_ready, DVE_LO)
                normalise(0, j, False, j > 2)
            with pool.Fori(1, GROUPS) as g:
                for j in range(SLOTS):
                    normalise(g, j, True, True)

            def output(back, j, loaded, made=carry_ready):
                done = SLOTS * back + SLOTS - j
                if loaded:
                    pool.wait_ge(x_loaded[j], 16 * (GROUPS - 1 + back))
                for k in range(K):
                    pool.wait_ge(made, K * (H - 2 + done) + k + 1)
                    pool.tensor_tensor(tile(x_ring, j, k), tile(x_ring, j, k), tile(d_ring, j, k),
                                       ALU.add).then_inc(out_ready, 1)

            for j in reversed(range(SLOTS)):
                output(0, j, False)
            with pool.Fori(1, GROUPS - 1) as back:
                for j in reversed(range(SLOTS)):
                    output(back, j, True)
            for j in reversed(range(1, SLOTS)):
                output(GROUPS - 1, j, True)
            output(GROUPS - 1, 0, True, row_ready)

        @block.scalar
        def _(act):
            act.dma_start(bias_sb[:, :], bias).then_inc(bias_loaded, 16)
            act.wait_ge(const_ready, 1)
            act.activation(table_probe[:, :], eps[:, 0:1], ACT.Sqrt)
            for k in range(2):
                act.wait_ge(w_loaded[k], 16)
                act.activation(w_hi[:, k, :], w_raw[k], ACT.Copy).then_inc(w_hi_ready, 1)
            act.wait_ge(var_summed, 1)
            act.activation(gn_std[:, :], bank[1][:, 0:K * NI], ACT.Sqrt, bias=eps[:, 0:1]).then_inc(std_ready, 1)
            for k in range(2, K):
                act.wait_ge(w_loaded[k], 16)
                act.activation(w_hi[:, k, :], w_raw[k], ACT.Copy).then_inc(w_hi_ready, 1)
            act.wait_ge(bias_loaded, 16)

            with act.Fori(0, STEPS) as s:
                for m in range(K):
                    act.wait_ge(psum_ready, K * s + m + 1)
                    act.activation(act_part[:, m, :], bank[m][:, COLS:2 * COLS], ACT.Identity,
                                   bias=bias_sb[:, m:m + 1]).then_inc(act_ready, 1)

        @block.vector
        def _(dve):
            dve.memset(group_avg[:, :], 0.0).then_inc(bn_step, 1)
            dve.wait_ge(bn_step, 1)
            for q in range(0, P, GN_GROUP):
                dve.memset(group_avg[q:q + GN_GROUP, q:q + GN_GROUP], 1.0 / GN_GROUP)
            dve.memset(eps[:, :], GN_EPS).then_inc(const_ready, 1)

            def channel_stats(ring, g, tiles):
                for i in range(tiles.start * NI, tiles.stop * NI):
                    last = dve.bn_stats(bn[:, i, g * BN_DIM:(g + 1) * BN_DIM], ring[:, :, i * WIDTH:(i + 1) * WIDTH])
                return last

            for g in range(LAST):
                for c in range(STAT_CHUNKS):
                    dve.wait_ge(stat_loaded[g % 2][c], 16 * (g // 2 + 1))
                    channel_stats((d_ring, x_ring)[g % 2], g, range(c * TC, (c + 1) * TC)).then_inc(stats_done, 1)

            def channel_moments(k):
                dve.wait_ge(stats_done, LAST * STAT_CHUNKS + k + 1)
                for i in range(k * NI, (k + 1) * NI):
                    last = dve.bn_aggr(moments[:, i, :], bn[:, i, :])
                last.then_inc(moments_ready, 1)

            for k in range(K):
                dve.wait_ge(last_loaded[k], 16)
                channel_stats(x_ring, LAST, range(k, k + 1)).then_inc(stats_done, 1)
                if k >= 1:
                    channel_moments(k - 1)
            channel_moments(K - 1)
            dve.wait_ge(mean_summed, 1)
            dve.tensor_copy(gn_mean[:, :], bank[0][:, 0:K * NI]).then_inc(bn_step, 1)
            dve.wait_ge(bn_step, 2)
            dve.wait_ge(moments_ready, K)
            dve.tensor_tensor(delta[:, :], moments[:, :, 0], gn_mean[:, :], ALU.subtract).then_inc(bn_step, 1)
            dve.wait_ge(bn_step, 3)
            dve.tensor_tensor(spread[:, :], delta[:, :], delta[:, :], ALU.mult).then_inc(bn_step, 1)
            dve.wait_ge(bn_step, 4)
            dve.tensor_tensor(spread[:, :], spread[:, :], moments[:, :, 1], ALU.add).then_inc(spread_ready, 1)
            dve.wait_ge(std_ready, 1)
            dve.reciprocal(gn_rstd[:, :], gn_std[:, :]).then_inc(gn_ready, 1)

            def split(row, parity, j, m):
                dve.wait_ge(row_ready, K * row + m + 1)
                dve.tensor_copy(carry[:, parity, m, 0, :], tile(d_ring, j, m)).then_inc(hi_ready, 1)
                dve.wait_ge(hi_ready, K * row + m + 1)
                dve.tensor_tensor(carry[:, parity, m, 1, :], tile(d_ring, j, m),
                                  carry[:, parity, m, 0, :].bitcast(F32), ALU.subtract).then_inc(carry_ready, 1)

            dve.wait_ge(gn_ready, 1)
            for m in range(K):
                for i in range(m * NI, (m + 1) * NI):
                    cols = slice(i * WIDTH, (i + 1) * WIDTH)
                    last = dve.tensor_scalar(d_ring[:, 0, cols], x_ring[:, 0, cols], gn_mean[:, i:i + 1],
                                             gn_rstd[:, i:i + 1], ALU.subtract, ALU.mult)
                last.then_inc(row_ready, 1)
                split(0, 0, 0, m)

            for k in range(K - DVE_LO, K):
                dve.wait_ge(w_hi_ready, k + 1)
                dve.tensor_tensor(w_lo[:, k, :], w_raw[k], w_hi[:, k, :].bitcast(F32),
                                  ALU.subtract).then_inc(w_lo_rest_ready, 1)

            def tile_of(ring, slot):
                return lambda m: tile(ring, slot, m)

            def row_tiles(row, j, parity, addend, xn_before=None, last=False):
                for m in range(K):
                    n = K * (row - 1) + m
                    dve.wait_ge(act_ready, n + 1)
                    dve.tensor_tensor(summed[:, m % 2, :], bank[m][:, 0:COLS], act_part[:, m, :],
                                      ALU.add).then_inc(sum_ready, 1)
                    dve.wait_ge(sum_ready, n + 1)
                    if xn_before is not None:
                        dve.wait_ge(xn_ready, xn_before + m + 1)
                    dve.scalar_tensor_tensor(out=tile(d_ring, j, m), in0=summed[:, m % 2, :], scalar=0.0,
                                             in1=addend(m), op0=ALU.max, op1=ALU.add).then_inc(row_ready, 1)
                    if not last:
                        split(row, parity, j, m)

            def down_row(g, j, reused):
                h = SLOTS * g + j
                if reused:
                    dve.wait_ge(d_stored[j], 16 * g)
                row_tiles(h, j, j % 2, tile_of(xn, j % 2), K * (h - 1))

            for j in range(1, SLOTS):
                down_row(0, j, False)
            with dve.Fori(1, GROUPS) as g:
                for j in range(SLOTS):
                    down_row(g, j, True)

            def up_row(back, j, loaded, last=False):
                row = H - 1 + SLOTS * back + SLOTS - 1 - j
                if loaded:
                    dve.wait_ge(d_loaded[j], 16 * back)
                row_tiles(row, j, j % 2, tile_of(d_ring, j), last=last)

            for j in reversed(range(SLOTS - 1)):
                up_row(0, j, False)
            with dve.Fori(1, GROUPS - 1) as back:
                for j in reversed(range(SLOTS)):
                    up_row(back, j, True)
            for j in reversed(range(1, SLOTS)):
                up_row(GROUPS - 1, j, True)
            up_row(GROUPS - 1, 0, True, last=True)

        @block.tensor
        def _(pe):
            pe.wait_ge(const_ready, 1)
            pe.wait_ge(moments_ready, K)
            pe.matmul(bank[0][:, 0:K * NI], group_avg[:, :], moments[:, :, 0],
                      start=True, stop=True).then_inc(mean_summed, 1)
            pe.wait_ge(spread_ready, 1)
            pe.matmul(bank[1][:, 0:K * NI], group_avg[:, :], spread[:, :],
                      start=True, stop=True).then_inc(var_summed, 1)

            def product(parity, m, k):
                out_cols = slice(m * P, (m + 1) * P)
                pe.matmul(bank[m][:, 0:2 * COLS], w_hi[:, k, out_cols],
                          carry[:, parity, k, :, :].rearrange("p s c -> p (s c)"), start=(k == 0), stop=False)
                last = pe.matmul(bank[m][:, 0:COLS], w_lo[:, k, out_cols], carry[:, parity, k, 0, :],
                                 start=False, stop=(k == K - 1))
                if k == K - 1:
                    last.then_inc(psum_ready, 1)

            for k in range(WAVE):
                pe.wait_ge(w_lo_ready, k + 1)
                pe.wait_ge(carry_ready, k + 1)
                for m in range(K):
                    product(0, m, k)
            pe.wait_ge(w_lo_rest_ready, DVE_LO)
            pe.wait_ge(carry_ready, K)
            for m in range(K):
                for k in range(WAVE, K):
                    product(0, m, k)
            for t in range(WAVE_1):
                pe.wait_ge(carry_ready, K + t + 1)
                for m in range(t):
                    product(1, m, t)
                for k in range(t + 1):
                    product(1, t, k)
            pe.wait_ge(carry_ready, 2 * K)
            for m in range(WAVE_1):
                for k in range(WAVE_1, K):
                    product(1, m, k)
            for m in range(WAVE_1, K):
                for k in range(K):
                    product(1, m, k)

            with pe.Fori(1, STEPS // 2) as pair:
                for parity in range(2):
                    done = K * (2 * pair + parity)
                    pe.wait_ge(carry_ready, done + K - 2)
                    for k in range(K - 2):
                        product(parity, 0, k)
                    pe.wait_ge(carry_ready, done + K - 1)
                    product(parity, 0, K - 2)
                    for k in range(K - 1):
                        product(parity, 1, k)
                    pe.wait_ge(carry_ready, done + K)
                    product(parity, 0, K - 1)
                    product(parity, 1, K - 1)
                    for m in range(2, K):
                        for k in range(K):
                            product(parity, m, k)


def kernel(x, L0_conv_W, L0_conv_b):
    import concourse.bacc as bacc
    from concourse.bass_utils import run_bass_kernel_spmd

    x, w, b = np.asarray(x), np.asarray(L0_conv_W), np.asarray(L0_conv_b)
    N, C, H, W = x.shape
    K = C // P
    tap = (w.shape[2] - 1) // 2
    x_rows = np.ascontiguousarray(x.reshape(N, K, P, H, W).transpose(3, 2, 1, 0, 4)).reshape(H, P, K * N * W)
    w_t = np.ascontiguousarray(w[:, :, tap, 0].T).reshape(K, P, C)
    bias = np.ascontiguousarray(b.reshape(K, P).T)

    nc = bacc.Bacc("TRN2", target_bir_lowering=False, num_devices=1)
    arrays = {"x_rows": x_rows, "w_t": w_t, "bias": bias}
    ins = [nc.dram_tensor(name, a.shape, F32, kind="ExternalInput").ap() for name, a in arrays.items()]
    down_rows = nc.dram_tensor("down_rows", x_rows.shape, F32, kind="Internal").ap()
    out_rows = nc.dram_tensor("out_rows", x_rows.shape, F32, kind="ExternalOutput").ap()
    build(nc, *ins, down_rows, out_rows)
    got = run_bass_kernel_spmd(nc, [arrays], core_ids=[0]).results[0]["out_rows"]
    return np.ascontiguousarray(got.reshape(H, P, K, N, W).transpose(3, 2, 1, 0, 4)).reshape(N, C, H, W)
```
